# Optimizing a Trainium2 kernel written in Bass

```python
import numpy as np
import jax
import jax.numpy as jnp

def _softmax(x, axis=-1):
    return jax.nn.softmax(x, axis=axis)

def _gelu(x):
    return jax.nn.gelu(x, approximate=True)

def _silu(x):
    return jax.nn.silu(x)

def _sigmoid(x):
    return jax.nn.sigmoid(x)

def _layernorm(x, axis=-1, eps=1e-05):
    m = jnp.mean(x, axis=axis, keepdims=True)
    v = jnp.var(x, axis=axis, keepdims=True)
    return (x - m) / jnp.sqrt(v + eps)

def _scatter_add(tgt, idx, src, axis=0):
    return tgt.at[idx].add(src)

def _segment_sum(src, seg, n):
    return jax.ops.segment_sum(src, seg, n)
kernel_name = 'mk_conv_attn_hybrid_d2_conv_nhwc512_r4_845c35'

def setup_inputs(seed: int=0):
    np.random.seed(seed)
    _w = jnp.asarray

    def _rec_inputs():
        import jax
        import jax.numpy as jnp
        _gk = jax.random.key(seed)
        x = -0.0001538 + 1 * jax.random.normal(jax.random.fold_in(_gk, 1), (16, 16, 48, 128), jnp.float32)
        return x
    x = _rec_inputs()

    def _L0_conv_setup():
        import jax, jax.numpy as jnp
        import numpy as np
        import math
        H = 8
        MAX_POS = 48
        MAX_PART = 16

        def _rel_bias(table, L, max_len):
            b = table[max_len - L:max_len + L - 1]
            idx = jnp.arange(L)
            rel = idx[None, :] - idx[:, None] + (L - 1)
            return jnp.transpose(b[rel], (2, 0, 1))
        key = jax.random.key(seed)
        ks = jax.random.split(key, 7)
        B, N, T, C = (16, 16, 48, 128)
        s = 0.02
        return {'x': jax.random.normal(ks[0], (B, N, T, C), jnp.float32), 'Wq': jax.random.normal(ks[1], (C, C), jnp.float32) * s, 'Wk': jax.random.normal(ks[2], (C, C), jnp.float32) * s, 'Wv': jax.random.normal(ks[3], (C, C), jnp.float32) * s, 'Wo': jax.random.normal(ks[4], (C, C), jnp.float32) * s, 'rel_pos_bias': jax.random.normal(ks[5], (2 * MAX_POS - 1, H), jnp.float32) * s, 'particle_rel_pos_bias': jax.random.normal(ks[6], (2 * MAX_PART - 1, H), jnp.float32) * s}
    _L0_conv_all = _L0_conv_setup()
    _L0_conv_in = {k: v for k, v in _L0_conv_all.items() if k in ('Wq', 'Wk', 'Wv', 'Wo', 'rel_pos_bias', 'particle_rel_pos_bias')}
    del _L0_conv_all

    def _L1_attn_setup():
        import jax, jax.numpy as jnp
        import numpy as np
        EMBED = 128
        HID = 16
        BATCH = 4
        SEQ = 256
        key = jax.random.key(seed)
        ks = jax.random.split(key, 8)
        e, h = (EMBED, HID)
        inputs = jax.random.normal(ks[0], (BATCH, SEQ, e), dtype=jnp.float32)
        Wq = jax.random.normal(ks[1], (e, e), dtype=jnp.float32) / np.sqrt(e)
        Wk = jax.random.normal(ks[2], (e, e), dtype=jnp.float32) / np.sqrt(e)
        Wv = jax.random.normal(ks[3], (e, e), dtype=jnp.float32) / np.sqrt(e)
        W1 = jax.random.normal(ks[4], (h, 2 * e), dtype=jnp.float32) / np.sqrt(2 * e)
        b1 = jnp.zeros((h,), dtype=jnp.float32)
        w2 = jax.random.normal(ks[5], (h,), dtype=jnp.float32) / np.sqrt(h)
        b2 = jnp.zeros((1,), dtype=jnp.float32)
        return {'inputs': inputs, 'Wq': Wq, 'Wk': Wk, 'Wv': Wv, 'W1': W1, 'b1': b1, 'w2': w2, 'b2': b2}
    _L1_attn_all = _L1_attn_setup()
    _L1_attn_in = {k: v for k, v in _L1_attn_all.items() if k in ('Wq', 'Wk', 'Wv', 'W1', 'b1', 'w2', 'b2')}
    del _L1_attn_all

    def _L1_ffn_setup():
        import jax, jax.numpy as jnp
        import numpy as np
        import math
        B, T, D = (4, 2048, 128)
        E, K, F = (8, 2, 512)
        CAP_FACTOR = 1.25
        key = jax.random.key(seed)
        ks = jax.random.split(key, 4)
        return {'x': jax.random.normal(ks[0], (B, T, D), jnp.float32), 'gate_w': jax.random.normal(ks[1], (E, D), jnp.float32) * 0.01, 'w1': jax.random.normal(ks[2], (E, D, F), jnp.float32) * (1.0 / np.sqrt(D)), 'b1': jnp.zeros((E, F), jnp.float32), 'w2': jax.random.normal(ks[3], (E, F, D), jnp.float32) * (1.0 / np.sqrt(F)), 'b2': jnp.zeros((E, D), jnp.float32)}
    _L1_ffn_all = _L1_ffn_setup()
    _L1_ffn_in = {k: v for k, v in _L1_ffn_all.items() if k in ('gate_w', 'w1', 'b1', 'w2', 'b2')}
    del _L1_ffn_all
    return {'x': x, 'L0_conv_Wq': _L0_conv_in['Wq'], 'L0_conv_Wk': _L0_conv_in['Wk'], 'L0_conv_Wv': _L0_conv_in['Wv'], 'L0_conv_Wo': _L0_conv_in['Wo'], 'L0_conv_rel_pos_bias': _L0_conv_in['rel_pos_bias'], 'L0_conv_particle_rel_pos_bias': _L0_conv_in['particle_rel_pos_bias'], 'L1_attn_Wq': _L1_attn_in['Wq'], 'L1_attn_Wk': _L1_attn_in['Wk'], 'L1_attn_Wv': _L1_attn_in['Wv'], 'L1_attn_W1': _L1_attn_in['W1'], 'L1_attn_b1': _L1_attn_in['b1'], 'L1_attn_w2': _L1_attn_in['w2'], 'L1_attn_b2': _L1_attn_in['b2'], 'L1_ffn_gate_w': _L1_ffn_in['gate_w'], 'L1_ffn_w1': _L1_ffn_in['w1'], 'L1_ffn_b1': _L1_ffn_in['b1'], 'L1_ffn_w2': _L1_ffn_in['w2'], 'L1_ffn_b2': _L1_ffn_in['b2']}

def reference(x, L0_conv_Wq, L0_conv_Wk, L0_conv_Wv, L0_conv_Wo, L0_conv_rel_pos_bias, L0_conv_particle_rel_pos_bias, L1_attn_Wq, L1_attn_Wk, L1_attn_Wv, L1_attn_W1, L1_attn_b1, L1_attn_w2, L1_attn_b2, L1_ffn_gate_w, L1_ffn_w1, L1_ffn_b1, L1_ffn_w2, L1_ffn_b2):
    import jax
    import jax.numpy as jnp

    def _L0_conv_ref(x, Wq, Wk, Wv, Wo, rel_pos_bias, particle_rel_pos_bias):
        import jax, jax.numpy as jnp
        import numpy as np
        import math
        H = 8
        MAX_POS = 48
        MAX_PART = 16

        def _rel_bias(table, L, max_len):
            b = table[max_len - L:max_len + L - 1]
            idx = jnp.arange(L)
            rel = idx[None, :] - idx[:, None] + (L - 1)
            return jnp.transpose(b[rel], (2, 0, 1))
        B, N, T, C = x.shape
        hd = C // H
        L = N * T
        xf = x.reshape(B, L, C)
        q = (xf @ Wq).reshape(B, L, H, hd).transpose(0, 2, 1, 3)
        k = (xf @ Wk).reshape(B, L, H, hd).transpose(0, 2, 1, 3)
        v = (xf @ Wv).reshape(B, L, H, hd).transpose(0, 2, 1, 3)
        att = jnp.einsum('bhqd,bhkd->bhqk', q, k) * (1.0 / math.sqrt(hd))
        att = att.reshape(B, H, N, T, N, T)
        bias_t = _rel_bias(rel_pos_bias, T, MAX_POS).reshape(1, H, 1, T, 1, T)
        bias_p = _rel_bias(particle_rel_pos_bias, N, MAX_PART).reshape(1, H, N, 1, N, 1)
        att = att + bias_t + bias_p
        causal = jnp.tril(jnp.ones((T, T), dtype=bool))
        att = jnp.where(causal[None, None, None, :, None, :], att, -jnp.inf)
        att = jax.nn.softmax(att.reshape(B, H, L, L), axis=-1)
        y = att @ v
        y = y.transpose(0, 2, 1, 3).reshape(B, L, C) @ Wo
        return y.reshape(B, N, T, C)

    def _L1_attn_ref(inputs, Wq, Wk, Wv, W1, b1, w2, b2):
        import jax, jax.numpy as jnp
        import numpy as np
        EMBED = 128
        HID = 16
        BATCH = 4
        SEQ = 256
        e = inputs.shape[-1]
        q = jnp.einsum('bse,fe->bsf', inputs, Wq)
        k = jnp.einsum('bse,fe->bsf', inputs, Wk)
        v = jnp.einsum('bse,fe->bsf', inputs, Wv)
        A = jnp.einsum('bse,he->bsh', q, W1[:, :e]) + b1
        B = jnp.einsum('bse,he->bsh', k, W1[:, e:])
        hidden = jnp.tanh(A[:, :, None, :] + B[:, None, :, :])
        logits = jnp.einsum('bijh,h->bij', hidden, w2) + b2[0]
        attn = jax.nn.softmax(logits, axis=-1)
        return jnp.einsum('bij,bjd->bid', attn, v)

    def _L1_ffn_ref(x, gate_w, w1, b1, w2, b2):
        import jax, jax.numpy as jnp
        import numpy as np
        import math
        B, T, D = (4, 2048, 128)
        E, K, F = (8, 2, 512)
        CAP_FACTOR = 1.25
        Bx, Tx, Dx = x.shape
        N = Bx * Tx
        C = math.ceil(CAP_FACTOR * N / E)
        xf = x.reshape(N, Dx)
        probs = jax.nn.softmax(xf @ gate_w.T, axis=-1)
        topk_vals, topk_idx = jax.lax.top_k(probs, K)
        topk_vals = topk_vals / topk_vals.sum(-1, keepdims=True)
        flat_e = topk_idx.reshape(N * K)
        onehot = jax.nn.one_hot(flat_e, E, dtype=jnp.int32)
        pos = jnp.cumsum(onehot, axis=0)[jnp.arange(N * K), flat_e] - 1
        keep = pos < C
        pos_safe = jnp.where(keep, pos, C)
        token_ids = jnp.repeat(jnp.arange(N), K)
        buf = jnp.zeros((E, C + 1, Dx), x.dtype).at[flat_e, pos_safe].set(xf[token_ids])
        expert_in = buf[:, :C]
        h = jax.nn.gelu(jnp.einsum('ecd,edf->ecf', expert_in, w1) + b1[:, None, :], approximate=False)
        expert_out = jnp.einsum('ecf,efd->ecd', h, w2) + b2[:, None, :]
        gathered = expert_out[flat_e, jnp.minimum(pos_safe, C - 1)]
        w = (topk_vals.reshape(N * K) * keep).astype(x.dtype)
        out = (gathered * w[:, None]).reshape(N, K, Dx).sum(axis=1)
        return out.reshape(Bx, Tx, Dx)

    def _gn(v, G=32, eps=1e-05):
        B_, H_, W_, C_ = v.shape
        g = v.reshape(B_, H_, W_, G, C_ // G)
        m = jnp.mean(g, axis=(1, 2, 4), keepdims=True)
        s = jnp.var(g, axis=(1, 2, 4), keepdims=True)
        return ((g - m) / jnp.sqrt(s + eps)).reshape(v.shape)

    def _ln_c(v, eps=1e-06):
        m = jnp.mean(v, axis=-1, keepdims=True)
        s = jnp.var(v, axis=-1, keepdims=True)
        return (v - m) / jnp.sqrt(s + eps)

    def _ln_t(v, eps=1e-05):
        m = jnp.mean(v, axis=-1, keepdims=True)
        s = jnp.var(v, axis=-1, keepdims=True)
        return (v - m) / jnp.sqrt(s + eps)

    def _to_tokens(v):
        B_, H_, W_, C_ = v.shape
        return v.reshape(B_, H_ * W_, C_)

    def _from_tokens(t, like):
        return t.reshape(like.shape)
    x = x + _L0_conv_ref(_gn(x), L0_conv_Wq, L0_conv_Wk, L0_conv_Wv, L0_conv_Wo, L0_conv_rel_pos_bias, L0_conv_particle_rel_pos_bias)
    t = _to_tokens(x)
    t = t + _L1_attn_ref(_ln_t(t), L1_attn_Wq, L1_attn_Wk, L1_attn_Wv, L1_attn_W1, L1_attn_b1, L1_attn_w2, L1_attn_b2)
    t = t + _L1_ffn_ref(_ln_t(t), L1_ffn_gate_w, L1_ffn_w1, L1_ffn_b1, L1_ffn_w2, L1_ffn_b2)
    x = _from_tokens(t, x)
    return x

_drawn_inputs = setup_inputs


def setup_inputs(seed=0):
    import zlib

    import numpy as np

    out = dict(_drawn_inputs(seed))
    spreads = {'L1_attn_b1': (0.0, 0.412), 'L1_ffn_b1': (0.0, 0.1), 'L1_ffn_b2': (0.0, 0.1)}
    factors = {'L0_conv_Wq': 8.0,
     'L0_conv_Wk': 8.0,
     'L0_conv_rel_pos_bias': 25.833,
     'L0_conv_particle_rel_pos_bias': 26.069}
    for name, (base, spread) in spreads.items():
        noise = np.random.default_rng([zlib.crc32(name.encode()), seed]).standard_normal(out[name].shape)
        drawn = base * np.exp(spread * noise) if base else spread * noise
        out[name] = jnp.asarray(drawn.astype(out[name].dtype))
    for name, factor in factors.items():
        out[name] = (out[name] * factor).astype(out[name].dtype)
    return out
```

```python
import concourse.bass as bass
from concourse import mybir
from contextlib import ExitStack
from math import ceil

F32 = mybir.dt.float32
BF16 = mybir.dt.bfloat16
I32 = mybir.dt.int32
ALU = mybir.AluOpType
ACT = mybir.ActivationFunctionType
AX = mybir.AxisListType

P = 128
H, HD = 8, 16
HID = 16
E, F = 8, 512
MASKED = -1e30
NOWHERE = 1 << 22
ROW = 132
TICKS = 24

HALF = 384


def score_steps(nb_blocks):
    steps = []
    for quad in range(2):
        for lo in (0, HALF):
            for kb in range((lo + HALF) // P):
                q0 = max(lo, kb * P)
                steps.append((quad, lo, kb, q0, lo + HALF - q0))
    return steps


STEPS = score_steps(6)
LAST_OF_GROUP = [d for d, s in enumerate(STEPS) if d + 1 == len(STEPS) or STEPS[d + 1][:2] != s[:2]]

AUX = {t: [] for t in range(TICKS)}
for _s in range(6):
    _stage, _at = ("add", 4 * _s) if _s < 5 else ("end", -4)
    AUX[_at + 5] += [(_stage, "probsT", (_s, 0)), (_stage, "probsT", (_s, 1))]
    AUX[_at + 6] += [(_stage, "attended", _s)]
AUX[1] += [("in", "xT", 0), ("in", "xT", 1)]
AUX[2] += [("in", "group_mean", 0)]
AUX[3] += [("in", "group_var", 0)]
AUX[5] += [("end", "normT", 0), ("end", "normT", 1)]
AUX[5] = [("in", "q", 0), ("in", "q", 1), ("in", "k", 0), ("in", "k", 1)] + AUX[5]
AUX[6] += [("end", "gate", 0), ("in", "v", 0), ("in", "v", 1)]
AUX[8] += [("end", "position", 0)]
AUX[14] += [("mid", "heads", 0)]
AUX[15] += [("mid", "heads", 1)]
AUX[16] += [("mid", "heads", 2)]
AUX[17] += [("mid", "headsT", 0)]
AUX[18] += [("mid", "project", 0)]
AUX[20] += [("mid", "heads", 3), ("mid", "heads", 4), ("mid", "heads", 5)]
AUX[21] += [("mid", "headsT", 1), ("mid", "project", 1)]
AUX[22] += [("mid", "x1T", 0), ("mid", "x1T", 1)]
AUX[23] += [("mid", "B", 0), ("mid", "B", 1), ("mid", "A", 0), ("mid", "A", 1), ("mid", "V", 0), ("mid", "V", 1),
            ("in", "maxT", 0)]

MAX_PARTS = [(qb, lo, n) for qb in range(4) for lo, n in ((0, P * (qb + 1)),)] + \
            [(4, lo, 320) for lo in (0, 320)] + [(5, lo, 256) for lo in (0, 256, 512)]
MAX_UNITS = [(h, *part) for h in range(H) for part in MAX_PARTS]
MAX_COUNTS = [5, 6, 6, 6, 6, 6, 6, 5, 5, 5, 4, 4, 4, 4]
MAX_AT = {t: range(0) for t in range(TICKS)}
for _i, _n in enumerate(MAX_COUNTS):
    MAX_AT[TICKS - len(MAX_COUNTS) + _i] = range(sum(MAX_COUNTS[:_i]), sum(MAX_COUNTS[:_i]) + _n)
RING = 3
PARTS = 5


def tick_order(t):
    units = [("in", "max", u) for u in MAX_AT[t]]
    uses = list(AUX[t])
    step = max(1, len(units) // max(1, len(uses)))
    out = []
    while units or uses:
        out += units[:step]
        units = units[step:]
        for _ in range(1 if len(uses) <= 3 else 2):
            if uses and not (uses[0][1] == "maxT" and units):
                out.append(uses.pop(0))
    n = len(out)
    return [out[n * i // PARTS:n * (i + 1) // PARTS] for i in range(PARTS)]


ORDER = [use for t in range(TICKS) for part in tick_order(t) for use in part]


def ring_uses(stages):
    return [use for use in ORDER if use[0] in stages]


def a_col(q, g):
    return 16 * (q // 4) + 4 * g + q % 4


class Pass:

    def __init__(self, b, stages, base, first_bank):
        self.b, self.stages, self.base, self.first_bank = b, stages, base, first_bank
        self.last = {"in": b + 2, "mid": b + 1, "add": b, "end": b - 1}
        self.uses = ring_uses(stages)

    def has(self, stage):
        return stage in self.stages

    def batch(self, stage):
        return self.last[stage]

    def number(self, use):
        return self.base + self.uses.index(use)

    def bank(self, use):
        return (self.first_bank + self.uses.index(use)) % RING


def positive(count):
    return not isinstance(count, int) or count > 0


def hybrid_kernel(nc, x, Wq0, Wk0, Wv0, Wo0, rel_t, rel_n, Wq1, Wk1, Wv1, W1, b1, w2, b2,
                  gate_w, ew1, eb1, ew2, eb2, out, capacity=None):
    NB, N, T, C = x.shape
    TB = T // 8
    L = N * T
    CAP = capacity or ceil(1.25 * NB * L / E)
    CHUNK = HALF
    CHUNKS = CAP // CHUNK
    assert CAP % CHUNK == 0 and C == P and L == TB * P

    ALL = ("in", "mid", "add", "end")

    def stages_of(b):
        return tuple(s for s, o in zip(ALL, (2, 1, 0, -1)) if 0 <= b + o < NB)

    first_full, last_full = 1, NB - 3
    bases, n = {}, 0
    for b in range(-2, NB + 1):
        bases[b] = n
        n += len(ring_uses(stages_of(b)))
    per_pass = len(ring_uses(ALL))
    assert per_pass % RING == 0

    def passes(eng, body):
        for b in range(-2, first_full):
            body(Pass(b, stages_of(b), bases[b], bases[b] % RING))
        with eng.Fori(first_full, last_full + 1) as b:
            body(Pass(b, ALL, (b - first_full) * per_pass + bases[first_full], bases[first_full] % RING))
        for b in range(last_full + 1, NB + 1):
            body(Pass(b, stages_of(b), bases[b], bases[b] % RING))

    out_rows = out.rearrange("b n t c -> (b n t) c")

    ctx = ExitStack()
    with ctx:
        def sb(name, shape, dt=F32):
            return ctx.enter_context(nc.sbuf_tensor(name, shape, dt))

        def sem(name):
            return ctx.enter_context(nc.semaphore(name))

        parts_dram = nc.dram_tensor("qk_parts", [2, P, 3, L], BF16).ap()
        rows_dram = nc.dram_tensor("expert_rows", [E * CAP, ROW], F32).ap()

        ident = sb("ident", [P, P])
        group_avg = sb("group_avg", [P, P])
        mask8 = sb("mask8", [P, 8])
        onehot_k = sb("onehot_k", [96, P], BF16)
        bias_q = sb("bias_q", [96, H, L], BF16)
        before_lt = sb("before_lt", [P, P], BF16)
        before_le = sb("before_le", [P, P], BF16)
        before_mid = sb("before_mid", [P, P], BF16)
        ones_bf = sb("ones_bf", [P, P], BF16)
        expert_ids = sb("expert_ids", [P, E])
        tie_rank = sb("tie_rank", [P, E])
        token_ids = sb("token_ids", [P, TB], I32)
        ids_int = sb("ids_int", [P, 40], I32)
        wq0, wk0, wv0, wo0 = (sb(n_, [P, P]) for n_ in ("wq0", "wk0", "wv0", "wo0"))
        wv1T = sb("wv1T", [P, P])
        map_a = sb("map_a", [P, P])
        map_b = sb("map_b", [P, P])
        b1_col = sb("b1_col", [P, 1])
        b2_col = sb("b2_col", [P, 1])
        w2_shifted = sb("w2_shifted", [P, 4, 32])
        gateT = sb("gateT", [P, E])
        eb1T = sb("eb1T", [P, E * 4])
        x_in = sb("x_in", [P, TB, P])
        xT = sb("xT", [P, L])
        gn_stats = sb("gn_stats", [P, 2, 6])
        gn_mv = sb("gn_mv", [P, 2])
        gn_small = sb("gn_small", [P, 8])
        xnT = sb("xnT", [P, L])
        qk_parts = sb("qk_parts_sb", [P, 2, 3, L], BF16)
        v_next = sb("v_next", [P, TB, P])
        q_max = sb("q_max", [112, H, L], BF16)
        k_max = sb("k_max", [112, H, L], BF16)
        neg_max = sb("neg_max", [P, P])
        max_halves = sb("max_halves", [P, H, len(MAX_PARTS)])
        max_parts = sb("max_parts", [H * TB, 3, P], BF16)
        qk_rest = [xT[:], x_in[:].rearrange("p b c -> p (b c)")]
        a_masked = xnT[:, 0:HALF]
        max_rest = xnT[0:H * TB, HALF:HALF + P]
        q_parts = sb("q_parts", [99, H, L], BF16)
        k_parts = sb("k_parts", [99, H, L], BF16)
        v_aug = sb("v_aug", [P, TB, H, 32])
        probs0 = sb("probs0", [P, 2, 4, HALF])
        headsT_raw = sb("headsT_raw", [P, 2, L])
        head_scale = sb("head_scale", [P, 2, H])
        heads = sb("heads", [P, TB, P])
        headsT = sb("headsT", [P, L])
        x1_next = sb("x1_next", [P, TB, P])
        ln_stats = sb("ln_stats", [P, TB, 6])
        ln_mv = sb("ln_mv", [P, TB, 2])
        ln_small = sb("ln_small", [P, 3, TB])
        x1n = heads
        x1nT = headsT
        a_next = sb("a_next", [P, L // 8])
        b_next = sb("b_next", [P, L])
        v1_next = sb("v1_next", [P, TB, P])
        a_cols = sb("a_cols", [P, L // 8])
        b_rep = sb("b_rep", [P, L])
        v1 = sb("v1", [P, TB, P])
        x1 = sb("x1", [P, TB, P])
        hidden = sb("hidden", [P, 3, 4, L])
        logit_bias = sb("logit_bias", [P, 3])
        probs1 = sb("probs1", [P, L])
        row_sum = sb("row_sum", [P, 1])
        row_scale = sb("row_scale", [P, 2])
        probs1T = sb("probs1T", [P, L])
        x2 = sb("x2", [P, TB, P])
        rows = sb("rows", [P, TB, ROW])
        x2nT = headsT
        rt = sb("rt", [P, 12, TB, E])
        rs = sb("rs", [P, 12, 2, TB])
        chosen = sb("chosen", [P, TB, E], BF16)
        counts = sb("counts", [P, E])
        slots = sb("slots", [P, 2, TB], I32)

        scores = ctx.enter_context(nc.psum_tensor("scores", [P, 2, 512], F32))
        logits = ctx.enter_context(nc.psum_tensor("logits", [P, 2, 512], F32))
        av_bank = ctx.enter_context(nc.psum_tensor("av_bank", [P, 512], F32))
        ring = ctx.enter_context(nc.psum_tensor("ring", [P, RING, 512], F32))

        weights_in = sem("weights_in")
        tables_in = sem("tables_in")
        copies_in = sem("copies_in")
        made = sem("made")
        setup_pe = sem("setup_pe")
        setup_dve = sem("setup_dve")
        setup_act = sem("setup_act")
        setup_pool = sem("setup_pool")
        sp_passed, pool_passed, act_passed = sem("sp_passed"), sem("pool_passed"), sem("act_passed")
        x_loaded = sem("x_loaded")
        mean_ready = sem("mean_ready")
        var_ready = sem("var_ready")
        xn_ready = sem("xn_ready")
        parts_ready = sem("parts_ready")
        parts_stored = sem("parts_stored")
        max_loaded = sem("max_loaded")
        max_done = sem("max_done")
        max_parts_ready = sem("max_parts_ready")
        score_loaded = sem("score_loaded")
        max_rows_loaded = sem("max_rows_loaded")
        v_aug_ready = sem("v_aug_ready")
        scores_filled = sem("scores_filled")
        scores_read = sem("scores_read")
        av_done = sem("av_done")
        av_copied = sem("av_copied")
        res_loaded = sem("res_loaded")
        x1n_ready = sem("x1n_ready")
        ab_ready = sem("ab_ready")
        v1_ready = sem("v1_ready")
        x1_kept = sem("x1_kept")
        sums_dve = sem("sums_dve")
        sums_pool = sem("sums_pool")
        tanh_done = sem("tanh_done")
        logits_added = sem("logits_added")
        max1_ready = sem("max1_ready")
        probs1_ready = sem("probs1_ready")
        x2_stored = sem("x2_stored")
        x2n_ready = sem("x2n_ready")
        gate_exp = sem("gate_exp")
        chosen_ready = sem("chosen_ready")
        slots_ready = sem("slots_ready")
        rows_sent = sem("rows_sent")
        ring_filled = sem("ring_filled")
        ring_read = sem("ring_read")

        w1_raw = hidden[0:HID, 0, 0, 0:2 * P]
        wq1_raw, wk1_raw, wv1_raw = (hidden[:, 0, 1, P * i:P * i + P] for i in range(3))
        w1T = hidden[:, 0, 2, 0:2 * HID].rearrange("p (a h) -> p a h", a=2)
        w1T_rep = hidden[:, 0, 3, 0:2 * P].rearrange("p (a r h) -> p a r h", a=2, r=8)
        gate_raw = hidden[0:E, 0, 1, 3 * P:4 * P]
        eb1_raw = hidden[0:32, 0, 1, 4 * P:5 * P]
        w2_col = hidden[:, 0, 2, 40:41]
        t_raw = xnT[0:96, 0:48 * H].rearrange("p (w h) -> p w h", h=H)
        n_raw = xnT[0:96, 48 * H:64 * H].rearrange("p (w h) -> p w h", h=H)
        t_rest = xT[0:96, 0:48 * H].rearrange("p (w h) -> p w h", h=H)
        n_rest = xT[0:96, 48 * H:64 * H].rearrange("p (w h) -> p w h", h=H)
        tn_hi = qk_parts[0:96, 0, 0, 0:64 * H].rearrange("p (w h) -> p w h", h=H)
        tn_mid = qk_parts[0:96, 0, 1, 0:64 * H].rearrange("p (w h) -> p w h", h=H)
        tn_lo = qk_parts[0:96, 0, 2, 0:64 * H].rearrange("p (w h) -> p w h", h=H)
        ct_raw = b_next[0:48, 0:48 * H].rearrange("p (w h) -> p w h", h=H)
        cn_raw = b_next[64:80, 0:16 * H].rearrange("p (w h) -> p w h", h=H)
        ct_wide = q_parts[0:48, :, :]
        cn_wide = q_parts[64:80, :, :]
        hot_t = k_parts[0:48, 0, :]
        hot_n = k_parts[64:80, 0, :]
        clear_row = probs1[:, 0:ROW]

        expert_w = [probs0[:, r].rearrange("p g l -> p (g l)") for r in range(2)]
        up_w = [w[:, 0:F] for w in expert_w]
        down_w = [w[:, F:2 * F].rearrange("p (j d) -> p j d", d=P) for w in expert_w]
        down_b = [v1[:, r, :] for r in range(2)]
        wide = [t_[:] for t_ in (xT, xnT, b_rep, b_next, headsT, probs1)] + \
               [t_[:].rearrange("p b c -> p (b c)") for t_ in (x1_next, heads, v_next, x1)]
        chunk_rows = [t_[:, 0:3 * ROW].rearrange("p (b c) -> p b c", b=3) for t_ in wide[0:2 * CHUNKS]]
        chunkT = [probs1T[:, HALF * r:HALF * r + HALF] for r in range(2)]
        gelu_out = [hidden[:, r, :, 0:HALF] for r in range(2)]
        chunk_out = [x_in[:, 3 * r:3 * r + 3, :] for r in range(2)]
        up_banks = [scores[:, 0, 0:HALF], scores[:, 1, 0:HALF], ring[:, 0, 0:HALF], ring[:, 1, 0:HALF]]
        expert_in = [sem(f"expert_in_{r}") for r in range(2)]
        rows_in = [sem(f"rows_in_{i}") for i in range(2 * CHUNKS)]
        rowsT_filled = sem("rowsT_filled")
        rowsT_copied = sem("rowsT_copied")
        up_filled = sem("up_filled")
        gelu_done = sem("gelu_done")
        down_filled = sem("down_filled")
        chunk_ready = sem("chunk_ready")
        chunk_added = [sem(f"chunk_added_{r}") for r in range(2)]

        def added_before(pair, n, r):
            return pair * (48 * CHUNKS) + 48 * sum(k % 2 == r for k in range(n))

        def expert_pairs(eng, body):
            body(0, 0)
            with eng.Fori(1, E // 2) as pair:
                body(pair, pair * 2)

        def expert_loads(sp):
            sp.wait_ge(rows_sent, 16 + 192 * NB)
            sp.sem_inc(sp_passed, 1)

            def body(pair, e0):
                for r in range(2):
                    ex = e0 + r
                    if positive(count := ex * CHUNKS - CHUNKS):
                        sp.wait_ge(down_filled, count)
                        sp.sem_inc(sp_passed, 1)
                    if positive(count := ex * CHUNKS - CHUNKS):
                        sp.wait_ge(chunk_ready, count)
                        sp.sem_inc(sp_passed, 1)
                    sp.dma_start(up_w[r], ew1[ex, :, :]).then_inc(expert_in[r], 16)
                    sp.dma_start(down_w[r], ew2[ex, :, :].rearrange("(j p) d -> p j d", p=P)).then_inc(expert_in[r], 16)
                    sp.dma_start(down_b[r], eb2[ex, :].unsqueeze(0).to_broadcast([P, P])).then_inc(expert_in[r], 16)
                    for i in range(CHUNKS):
                        m = ex * CHUNKS + i
                        n = r * CHUNKS + i
                        if positive(count := m - 2 * CHUNKS + 3):
                            sp.wait_ge(chunk_ready, count)
                            sp.sem_inc(sp_passed, 1)
                        sp.dma_start(chunk_rows[n], rows_dram[bass.ds(m * HALF, HALF), :]
                                     .rearrange("(b p) c -> p b c", p=P)).then_inc(rows_in[n], 16)

            expert_pairs(sp, body)
            for r in range(2):
                sp.wait_ge(chunk_added[r], 48 * E * CHUNKS // 2)

        def expert_products(pe):
            mm = nc.tensor.matmul

            def body(pair, e0):
                def transpose_rows(n):
                    m = e0 * CHUNKS + n
                    pe.wait_ge(rows_in[n], pair * 16 + 16)
                    if positive(count := m):
                        pe.wait_ge(rowsT_copied, count)
                    for j in range(3):
                        last = nc.tensor.transpose(av_bank[:, P * j:P * j + P], chunk_rows[n][:, j, 0:P],
                                                   ident[:])
                    last.then_inc(rowsT_filled, 1)

                def up(n):
                    m, r = e0 * CHUNKS + n, n // CHUNKS
                    if n % CHUNKS == 0:
                        pe.wait_ge(expert_in[r], pair * 48 + 48)
                    pe.wait_ge(rowsT_copied, m + 1)
                    for j in range(4):
                        if positive(count := m * 4 - 4 + (j + 1)):
                            pe.wait_ge(gelu_done, count)
                        mm(up_banks[j], up_w[r][:, P * j:P * j + P], chunkT[n % 2], start=True, stop=True) \
                            .then_inc(up_filled, 1)

                def down(n):
                    m, r = e0 * CHUNKS + n, n // CHUNKS
                    pe.wait_ge(gelu_done, m * 4 + 4)
                    if positive(count := m - 1):
                        pe.wait_ge(chunk_ready, count)
                    for b_ in range(3):
                        for j in range(4):
                            last = mm(logits[:, n % 2, P * b_:P * b_ + P], gelu_out[n % 2][:, j, P * b_:P * b_ + P],
                                      down_w[r][:, j, :], start=(j == 0), stop=(j == 3))
                    last.then_inc(down_filled, 1)

                for n in range(2 * CHUNKS + 1):
                    if n == 0:
                        transpose_rows(0)
                    if n + 1 < 2 * CHUNKS:
                        transpose_rows(n + 1)
                    if n < 2 * CHUNKS:
                        up(n)
                    if n > 0:
                        down(n - 1)

            expert_pairs(pe, body)

        def expert_gelu(act):
            def body(pair, e0):
                for n in range(2 * CHUNKS):
                    m = e0 * CHUNKS + n
                    if positive(count := m - 1):
                        act.wait_ge(down_filled, count)
                    for j in range(4):
                        act.wait_ge(up_filled, m * 4 + (j + 1))
                        act.sem_inc(act_passed, 1)
                        nc.scalar.activation(gelu_out[n % 2][:, j, :], up_banks[j], ACT.Gelu,
                                             bias=eb1T[:, bass.ds(e0 * 4 + (4 * (n // CHUNKS) + j), 1)]) \
                            .then_inc(gelu_done, 1)

            expert_pairs(act, body)

        def expert_vector(dve):
            v = nc.vector

            def body(pair, e0):
                def copy_rows(n):
                    m = e0 * CHUNKS + n
                    dve.wait_ge(rowsT_filled, m + 1)
                    if positive(count := m * 4 - 4):
                        dve.wait_ge(up_filled, count)
                    v.tensor_copy(chunkT[n % 2], av_bank[:, 0:HALF]).then_inc(rowsT_copied, 1)

                def weigh(n):
                    m, r = e0 * CHUNKS + n, n // CHUNKS
                    src = chunk_rows[n]
                    if n % CHUNKS == 0:
                        dve.wait_ge(expert_in[r], pair * 48 + 48)
                    dve.wait_ge(rows_in[n], pair * 16 + 16)
                    v.tensor_scalar(rs[:, 0, 0, 0:3], src[:, :, 130], expert_ids[:, bass.ds(e0 + r, 1)], None,
                                    ALU.is_equal)
                    v.tensor_tensor(rs[:, 1, 0, 0:3], src[:, :, 129], src[:, :, 131], ALU.subtract)
                    dve.drain()
                    v.tensor_tensor(rs[:, 2, 0, 0:3], rs[:, 0, 0, 0:3], rs[:, 1, 0, 0:3], ALU.mult)
                    dve.drain()
                    v.tensor_tensor(rs[:, 3, 0, 0:3], rs[:, 2, 0, 0:3], src[:, :, 131], ALU.add)
                    dve.wait_ge(down_filled, m + 1)
                    if positive(count := added_before(pair, n, n % 2)):
                        dve.wait_ge(chunk_added[n % 2], count)
                    v.tensor_tensor(chunk_out[n % 2], logits[:, n % 2, 0:HALF].rearrange("p (b c) -> p b c", b=3),
                                    down_b[r].unsqueeze(1).to_broadcast([P, 3, P]), ALU.add)
                    dve.drain()
                    for b_ in range(3):
                        v.tensor_scalar(chunk_out[n % 2][:, b_, :], chunk_out[n % 2][:, b_, :],
                                        rs[:, 3, 0, b_:b_ + 1], None, ALU.mult)
                    dve.drain()
                    v.memset(gn_small[:, 6:7], 0.0).then_inc(chunk_ready, 1)

                for n in range(2 * CHUNKS + 1):
                    if n == 0:
                        copy_rows(0)
                    if n + 1 < 2 * CHUNKS:
                        copy_rows(n + 1)
                    if n > 0:
                        weigh(n - 1)

            expert_pairs(dve, body)

        def expert_scatter(pool):
            pool.wait_ge(x2_stored, 96 * NB)
            pool.sem_inc(pool_passed, 1)

            def body(pair, e0):
                for n in range(2 * CHUNKS):
                    m = e0 * CHUNKS + n
                    pool.wait_ge(chunk_ready, m + 1)
                    pool.sem_inc(pool_passed, 1)
                    if n % CHUNKS == 0:
                        for r in range(2):
                            if positive(count := added_before(pair, n, r)):
                                pool.wait_ge(chunk_added[r], count)
                                pool.sem_inc(pool_passed, 1)
                    for b_ in range(3):
                        pool.indirect_dma_start(
                            out_rows, bass.IndirectOffsetOnAxis(chunk_rows[n][:, b_, 128:129].bitcast(I32), 0),
                            chunk_out[n % 2][:, b_, :], None, bounds_check=NB * L - 1, oob_is_err=False,
                            compute_op=ALU.add).then_inc(chunk_added[n % 2], 16)

            expert_pairs(pool, body)

        block = ctx.enter_context(nc.Block())

        @block.sync
        def _(sp):
            def load_x(c):
                for tb in range(TB):
                    sp.dma_start(x_in[:, tb, :], x[c, :, 8 * tb:8 * tb + 8, :]).then_inc(x_loaded, 16)

            sp.wait_ge(setup_dve, 1)
            for g in range(3):
                sp.dma_start(t_raw[32 * g:32 * g + 8], bass.AP(rel_t.tensor, rel_t.offset,
                                                               [[H, 8], [H, 48], [1, H]])).then_inc(tables_in, 16)
                sp.dma_start(n_raw[32 * g + 8:32 * g + 24], bass.AP(rel_n.tensor, rel_n.offset,
                                                                    [[H, 16], [H, 16], [1, H]])).then_inc(tables_in, 16)
            sp.dma_start(ct_raw, bass.AP(rel_t.tensor, rel_t.offset, [[H, 48], [H, 48], [1, H]])).then_inc(tables_in, 16)
            sp.dma_start(cn_raw, bass.AP(rel_n.tensor, rel_n.offset, [[H, 16], [H, 16], [1, H]])).then_inc(tables_in, 16)
            for dst, src in ((wq0[:], Wq0), (wk0[:], Wk0), (wv0[:], Wv0), (wo0[:], Wo0),
                             (wq1_raw, Wq1), (wk1_raw, Wk1), (wv1_raw, Wv1), (w1_raw, W1), (gate_raw, gate_w),
                             (eb1_raw, eb1.rearrange("e (j p) -> (e j) p", p=P)),
                             (b2_col[:], bass.AP(b2.tensor, b2.offset, [[0, P], [1, 1]]))):
                sp.dma_start(dst, src).then_inc(weights_in, 16)
            for r in range(8):
                sp.dma_start(b1_col[HID * r:HID * r + HID, :], b1.rearrange("(h o) -> h o", o=1)).then_inc(weights_in, 16)
                sp.dma_start(w2_col[HID * r:HID * r + HID, :], w2.rearrange("(h o) -> h o", o=1)).then_inc(weights_in, 16)
            load_x(0)
            sp.wait_ge(setup_pool, 1)
            for h in range(H):
                sp.dma_start(q_max[48:96, h, :], hot_t).then_inc(copies_in, 16)
                sp.dma_start(q_max[96:112, h, :], hot_n).then_inc(copies_in, 16)
            sp.dma_start(k_max[48:96, :, :], ct_wide).then_inc(copies_in, 16)
            sp.dma_start(k_max[96:112, :, :], cn_wide).then_inc(copies_in, 16)
            sp.wait_ge(copies_in, 16 * 18)
            for j in range(3):
                sp.dma_start(k_parts[96 + j:97 + j, :, :], q_parts[96:97, :, :]).then_inc(copies_in, 16)
            sp.wait_ge(copies_in, 16 * 21)

            def store_block(ps, stage, s):
                b = ps.batch(stage)
                sp.wait_ge(ring_read, ps.number((stage, "attended", s)) + 1)
                sp.sem_inc(sp_passed, 1)
                if positive(count := b * 96 + 16 * s):
                    sp.wait_ge(x2_stored, count)
                    sp.sem_inc(sp_passed, 1)
                sp.dma_start(out[b, :, 8 * s:8 * s + 8, :], x2[:, s, :]).then_inc(x2_stored, 16)

            def body(ps):
                for t in range(TICKS):
                    if ps.has("in"):
                        c = ps.batch("in")
                        if t == 0 and positive(count := c * 2):
                            sp.wait_ge(parts_ready, count)
                            sp.sem_inc(sp_passed, 1)
                            load_x(c)
                        if t == 7:
                            sp.wait_ge(parts_ready, c * 2 + 2)
                            sp.sem_inc(sp_passed, 1)
                            sp.dma_start(parts_dram.rearrange("w p j l -> p w j l"), qk_parts[:, :, :, :]) \
                              .then_inc(parts_stored, 16)
                            sp.wait_ge(parts_stored, c * 16 + 16)
                            sp.sem_inc(sp_passed, 1)
                            if positive(count := c):
                                sp.wait_ge(max_parts_ready, count)
                                sp.sem_inc(sp_passed, 1)
                            for dst, w, js in ((q_max, 0, (0, 0, 1)), (k_max, 1, (0, 1, 0))):
                                for i, j in enumerate(js):
                                    sp.dma_start(dst[16 * i:16 * i + 16, :, :],
                                                 parts_dram[w, :, j, :].rearrange("(h d) l -> d h l", d=HD)) \
                                      .then_inc(max_loaded, 16)
                        if t == 19:
                            if positive(count := c * 36):
                                sp.wait_ge(scores_filled, count)
                                sp.sem_inc(sp_passed, 1)
                            for dst, w, js in ((q_parts, 0, (0, 0, 1, 1, 0, 2)), (k_parts, 1, (0, 1, 0, 1, 2, 0))):
                                for i, j in enumerate(js):
                                    sp.dma_start(dst[16 * i:16 * i + 16, :, :],
                                                 parts_dram[w, :, j, :].rearrange("(h d) l -> d h l", d=HD)) \
                                      .then_inc(score_loaded, 16)
                            sp.wait_ge(score_loaded, c * 192 + 192)
                            sp.sem_inc(sp_passed, 1)
                            sp.wait_ge(max_loaded, c * 96 + 96)
                            sp.sem_inc(sp_passed, 1)
                        if t == 23:
                            sp.wait_ge(max_parts_ready, c + 1)
                            sp.sem_inc(sp_passed, 1)
                            for j in range(3):
                                sp.dma_start(q_parts[96 + j:97 + j, :, :], max_parts[:, j, :]) \
                                  .then_inc(max_rows_loaded, 16)
                    if ps.has("mid") and t == 5:
                        c = ps.batch("mid")
                        if positive(count := c):
                            sp.wait_ge(x1_kept, count)
                            sp.sem_inc(sp_passed, 1)
                        for tb in range(TB):
                            sp.dma_start(x1_next[:, tb, :], x[c, :, 8 * tb:8 * tb + 8, :]).then_inc(res_loaded, 16)
                    if ps.has("add") and t >= 6 and t % 4 == 2:
                        store_block(ps, "add", t // 4 - 1)
                    if ps.has("end") and t == 2:
                        store_block(ps, "end", 5)

            passes(sp, body)
            expert_loads(sp)

        @block.gpsimd
        def _(pool):
            g = nc.gpsimd
            for tile_ in (ident[:], group_avg[:], mask8[:], onehot_k[:], hot_t, hot_n, v_aug[:]):
                g.memset(tile_, 0.0)
                pool.drain()
            for tile_, v in ((before_lt[:], 1.0), (before_le[:], 1.0), (before_mid[:], 1.0), (ones_bf[:], 1.0),
                             (q_parts[96:99, :, :], 1.0), (neg_max[:], 0.0), (w2_shifted[:], 0.0), (counts[:], 0.0), (clear_row, 0.0)):
                g.memset(tile_, v)
                pool.drain()

            def select(tile_, op, fill, base, pattern, cm):
                g.affine_select(out=tile_, in_=tile_, compare_op=op, fill=fill, base=base, pattern=pattern,
                                channel_multiplier=cm)
                pool.drain()

            select(ident[:], ALU.not_equal, 1.0, 0, [[-1, P]], 1)
            g.memset(group_avg[:], 0.25)
            g.memset(mask8[:], 1.0)
            pool.drain()
            ga = group_avg[:].rearrange("p (j r) -> p j r", r=4)
            select(ga, ALU.is_ge, 0.0, 0, [[-4, 32], [0, 4]], 1)
            select(mask8[:], ALU.is_ge, 0.0, 0, [[-16, 8]], 1)
            pool.drain()
            select(ga, ALU.is_ge, 0.0, 3, [[4, 32], [0, 4]], -1)
            select(mask8[:], ALU.is_ge, 0.0, 15, [[16, 8]], -1)
            for q in range(3):
                v = onehot_k[32 * q:32 * q + 32, :].rearrange("p (n t) -> p n t", t=8)
                select(v, ALU.not_equal, 1.0, 0, [[0, 16], [1, 8]], -1)
            pool.drain()
            for q in range(3):
                v = onehot_k[32 * q:32 * q + 32, :].rearrange("p (n t) -> p n t", t=8)
                select(v, ALU.not_equal, 1.0, 8, [[1, 16], [0, 8]], -1)
            select(before_lt[:].rearrange("p (n t) -> p n t", t=8), ALU.is_ge, 0.0, -1, [[8, 16], [0, 8]], -1)
            select(before_le[:].rearrange("p (n t) -> p n t", t=8), ALU.is_ge, 0.0, 7, [[8, 16], [0, 8]], -1)
            select(before_mid[:], ALU.is_ge, 0.0, -1, [[1, P]], -1)
            select(hot_t.rearrange("p (b n t) -> p b n t", n=16, t=8), ALU.not_equal, 1.0, -47,
                   [[8, TB], [0, 16], [1, 8]], 1)
            select(hot_n.rearrange("p (b n t) -> p b n t", n=16, t=8), ALU.not_equal, 1.0, -15,
                   [[0, TB], [1, 16], [0, 8]], 1)
            g.memset(v_aug[:, :, :, 16:17], 1.0)
            g.iota(ids_int[:, 0:16], pattern=[[-8, 16]], base=0, channel_multiplier=1)
            g.iota(ids_int[:, 16:16 + TB], pattern=[[8, TB]], base=0, channel_multiplier=1)
            g.iota(ids_int[:, 24:32], pattern=[[1, E]], base=0, channel_multiplier=0)
            g.iota(ids_int[:, 32:40], pattern=[[-1, E]], base=E, channel_multiplier=0)
            g.memset(clear_row[:, 128:129].bitcast(I32), NOWHERE)
            pool.drain()
            g.memset(neg_max[:, 0:1], 0.0).then_inc(made, 1)
            pool.wait_ge(made, 1)
            pool.dma_start(rows_dram.rearrange("(a p) c -> p a c", p=P),
                           clear_row.unsqueeze(1).to_broadcast([P, E * CAP // P, ROW])).then_inc(rows_sent, 16)
            pool.wait_ge(setup_dve, 2)
            pool.wait_ge(setup_act, 1)
            for h in range(H):
                select(bias_q[0:8, h, 0:P].rearrange("p (n t) -> p n t", t=8), ALU.is_ge, MASKED, 0,
                       [[0, 16], [1, 8]], -1)
                select(ct_wide[:, h, :].rearrange("p (b n t) -> p b n t", n=16, t=8), ALU.is_ge, MASKED, 47,
                       [[-8, TB], [0, 16], [-1, 8]], -1)
            pool.drain()
            g.memset(neg_max[:, 1:2], 0.0).then_inc(setup_pool, 1)

            def sums(b, q):
                if positive(count := b * 24 + (q - 2)):
                    pool.wait_ge(logits_added, count)
                    pool.sem_inc(pool_passed, 1)
                for o in range(1, 3 if q < TICKS - 1 else 4):
                    last = g.tensor_scalar(hidden[:, q % 3, o, :], b_rep[:], 1.0,
                                           a_cols[:, a_col(q, o):a_col(q, o) + 1], ALU.mult, ALU.add)
                last.then_inc(sums_pool, 1)

            def body(ps):
                for t in range(TICKS):
                    if ps.has("add"):
                        b = ps.batch("add")
                        if t == 0:
                            pool.wait_ge(ab_ready, b + 1)
                            pool.sem_inc(pool_passed, 1)
                            sums(b, 0)
                        if t < TICKS - 1:
                            sums(b, t + 1)
                        if t == 3:
                            if ps.has("end"):
                                pool.wait_ge(ring_read, ps.number(("end", "attended", 5)) + 1)
                                pool.sem_inc(pool_passed, 1)
                            g.tensor_copy(v1[:], v1_next[:]).then_inc(v1_ready, 1)
                            g.tensor_copy(x1[:], x1_next[:]).then_inc(x1_kept, 1)
                    if ps.has("in"):
                        c = ps.batch("in")
                        if t == 6:
                            if positive(count := c * 16):
                                pool.wait_ge(parts_stored, count)
                                pool.sem_inc(pool_passed, 1)
                            for w in range(2):
                                use = ("in", ("q", "k")[w], 1)
                                pool.wait_ge(ring_read, ps.number(use) + 1)
                                pool.sem_inc(pool_passed, 1)
                                g.tensor_copy(qk_parts[:, w, 1, :], qk_rest[w])
                            pool.drain()
                            for w in range(2):
                                g.tensor_tensor(qk_parts[:, w, 2, :], qk_rest[w], qk_parts[:, w, 1, :],
                                                ALU.subtract).then_inc(parts_ready, 1)
                        if t == 21:
                            if positive(count := c * 18):
                                pool.wait_ge(av_done, count)
                                pool.sem_inc(pool_passed, 1)
                            pool.wait_ge(ring_read, ps.number(("in", "v", 1)) + 1)
                            pool.sem_inc(pool_passed, 1)
                            g.tensor_copy(v_aug[:, :, :, 0:16], v_next[:].rearrange("p b (h d) -> p b h d", d=HD)) \
                             .then_inc(v_aug_ready, 1)
                    if ps.has("end") and 10 <= t < 16:
                        c = ps.batch("end")
                        tb = t - 10
                        if t == 10:
                            pool.wait_ge(slots_ready, c + 1)
                            pool.sem_inc(pool_passed, 1)
                            pool.wait_ge(rows_sent, 16 + c * 192)
                            pool.sem_inc(pool_passed, 1)
                        for k in range(2):
                            pool.indirect_dma_start(rows_dram, bass.IndirectOffsetOnAxis(slots[:, k, tb:tb + 1], 0),
                                                    rows[:, tb, :], None, bounds_check=E * CAP - 1,
                                                    oob_is_err=False).then_inc(rows_sent, 16)

            passes(pool, body)
            expert_scatter(pool)

        @block.scalar
        def _(act):
            s = nc.scalar

            act.wait_ge(tables_in, 16 * 8)
            act.wait_ge(made, 1)
            for h in range(H):
                for tb in range(TB):
                    s.activation(ct_wide[:, h, P * tb:P * tb + P].rearrange("p (n t) -> p n t", t=8),
                                 ct_raw[:, 8 * tb:8 * tb + 8, h].unsqueeze(1).to_broadcast([48, 16, 8]), ACT.Copy)
                    s.activation(cn_wide[:, h, P * tb:P * tb + P].rearrange("p (n t) -> p n t", t=8),
                                 cn_raw[:, :, h].unsqueeze(2).to_broadcast([16, 16, 8]), ACT.Copy)
            act.drain()
            s.activation(logit_bias[:, 0:1], ids_int[:, 0:1], ACT.Copy).then_inc(setup_act, 1)

            def exp_scores(c, d, pair):
                n_ = STEPS[d][4]
                act.wait_ge(scores_filled, c * 36 + (2 * d + pair + 1))
                if pair == 0:
                    if positive(count := c * 18 + (d - 1)):
                        act.wait_ge(av_done, count)
                s.activation(probs0[:, d % 2, 2 * pair:2 * pair + 2, 0:n_], scores[:, :, 0:n_], ACT.Exp) \
                 .then_inc(scores_read, 1)

            def exp_logits(b, blk):
                if positive(count := b * 6 + (blk + 1)):
                    act.wait_ge(max1_ready, count)
                s.activation(probs1[:].rearrange("p (a k) -> p a k", a=2), logits[:, :, 0:HALF], ACT.Exp,
                             bias=logit_bias[:, 2:3], accum_out=row_sum[:]).then_inc(probs1_ready, 1)

            def body(ps):
                for t in range(TICKS):
                    d = t - 1
                    if ps.has("mid") and 0 <= d < len(STEPS):
                        exp_scores(ps.batch("mid"), d, 0)
                    if ps.has("add"):
                        b = ps.batch("add")
                        act.wait_ge(sums_dve, b * 24 + (t + 1))
                        act.wait_ge(sums_pool, b * 24 + (t + 1))
                        if t < TICKS - 1:
                            s.activation(hidden[:, t % 3, 0:3, :], hidden[:, t % 3, 0:3, :], ACT.Tanh)
                        else:
                            s.activation(hidden[:, t % 3, :, :], hidden[:, t % 3, :, :], ACT.Tanh) \
                             .then_inc(tanh_done, 1)
                    if ps.has("mid") and 0 <= d < len(STEPS):
                        exp_scores(ps.batch("mid"), d, 1)
                    if ps.has("add") and t < TICKS - 1:
                        col = a_col(t, 3)
                        s.activation(hidden[:, t % 3, 3, :], b_rep[:], ACT.Tanh, bias=a_cols[:, col:col + 1]) \
                         .then_inc(tanh_done, 1)
                    if ps.has("end") and t == 0:
                        exp_logits(ps.batch("end"), 5)
                    if ps.has("add") and t >= 4 and t % 4 == 0:
                        exp_logits(b, t // 4 - 1)
                    if ps.has("end"):
                        c = ps.batch("end")
                        if t == 6:
                            act.wait_ge(ring_read, ps.number(("end", "gate", 0)) + 1)
                            s.activation(rt[:, 1, :, :], rt[:, 0, :, :], ACT.Exp).then_inc(gate_exp, 1)

            passes(act, body)
            expert_gelu(act)

        @block.tensor
        def _(pe):
            mm = nc.tensor.matmul
            pe.wait_ge(made, 1)
            pe.wait_ge(weights_in, 16 * 27)
            nc.tensor.transpose(ring[:, 0, 0:P], wv1_raw, ident[:])
            nc.tensor.transpose(ring[:, 0, P:P + HID], w1_raw[:, 0:P], ident[0:HID, 0:HID])
            nc.tensor.transpose(ring[:, 0, P + HID:P + 2 * HID], w1_raw[:, P:2 * P], ident[0:HID, 0:HID])
            nc.tensor.transpose(ring[:, 0, 192:192 + E], gate_raw, ident[0:E, 0:E])
            nc.tensor.transpose(ring[:, 0, 256:288], eb1_raw, ident[0:32, 0:32]).then_inc(setup_pe, 1)
            pe.wait_ge(setup_dve, 3)
            mm(av_bank[:, 0:P], wq1_raw, w1T_rep[:, 0].rearrange("p r h -> p (r h)"), start=True, stop=True)
            mm(av_bank[:, P:2 * P], wk1_raw, w1T_rep[:, 1].rearrange("p r h -> p (r h)"),
               start=True, stop=True).then_inc(setup_pe, 1)
            pe.wait_ge(setup_dve, 4)

            def fill_scores(c, d, pair):
                quad, lo, kb, q0, n_ = STEPS[d]
                if d == 0 and pair == 0 and not positive(c):
                    pe.wait_ge(copies_in, 16 * 21)
                    pe.wait_ge(setup_pool, 1)
                if d == 0 and pair == 0:
                    pe.wait_ge(score_loaded, c * 192 + 192)
                    pe.wait_ge(max_rows_loaded, c * 48 + 48)
                if positive(count := c * 36 + (2 * d + pair)):
                    pe.wait_ge(scores_read, count)
                for j in range(2):
                    h = 4 * quad + 2 * pair + j
                    mm(scores[:, j, 0:n_], k_parts[0:99, h, P * kb:P * kb + P], q_parts[0:99, h, q0:q0 + n_],
                       start=True, stop=False)
                    last = mm(scores[:, j, 0:n_], onehot_k[:], bias_q[:, h, q0 - P * kb:q0 - P * kb + n_],
                              start=False, stop=True)
                last.then_inc(scores_filled, 1)

            def weigh_values(c, d):
                quad, lo, kb, q0, n_ = STEPS[d]
                pe.wait_ge(scores_read, c * 36 + (2 * d + 2))
                if d == 0:
                    pe.wait_ge(v_aug_ready, c + 1)
                if kb == 0:
                    group = sum(g < d for g in LAST_OF_GROUP)
                    if positive(count := c * 4 + group):
                        pe.wait_ge(av_copied, count)
                for g in range(4):
                    last = mm(av_bank[32 * g:32 * g + 32, q0 - lo:q0 - lo + n_], v_aug[:, kb, 4 * quad + g, :],
                              probs0[:, d % 2, g, 0:n_], start=(kb == 0), stop=(d in LAST_OF_GROUP))
                last.then_inc(av_done, 1)

            def add_logits(b, q, half):
                k = q % 4
                if half == 0:
                    pe.wait_ge(tanh_done, b * 24 + (q + 1))
                    if k == 0:
                        if positive(count := b * 6 + q // 4):
                            pe.wait_ge(probs1_ready, count)
                for g in range(4):
                    last = mm(logits[32 * g:32 * g + 32, half, 0:HALF], w2_shifted[:, k, :],
                              hidden[:, q % 3, g, HALF * half:HALF * half + HALF], start=(k == 0), stop=(k == 3))
                if half == 1:
                    last.then_inc(logits_added, 1)

            def fill(ps, use):
                stage, name, i = use
                c = ps.batch(stage)
                bank = ring[:, ps.bank(use)]

                def after(name_, i_):
                    pe.wait_ge(ring_read, ps.number((stage, name_, i_)) + 1)

                if name == "xT":
                    if i == 0:
                        pe.wait_ge(x_loaded, c * 96 + 96)
                elif name == "group_mean":
                    pe.wait_ge(mean_ready, c + 1)
                elif name == "group_var":
                    pe.wait_ge(var_ready, c + 1)
                elif name in ("q", "k", "v"):
                    pe.wait_ge(xn_ready, c + 1)
                elif name == "max":
                    if i == 0:
                        if not positive(c):
                            pe.wait_ge(copies_in, 16 * 21)
                        pe.wait_ge(max_loaded, c * 96 + 96)
                elif name == "maxT":
                    pe.wait_ge(max_done, c + 1)
                elif name == "heads":
                    pe.wait_ge(av_copied, c * 4 + (3 if i < 3 else 4))
                elif name == "headsT":
                    after("heads", 3 * i + 2)
                elif name == "project":
                    after("headsT", i)
                elif name == "x1T":
                    pe.wait_ge(x1n_ready, c + 1)
                elif name in ("A", "B", "V"):
                    after("x1T", 1)
                elif name == "probsT":
                    pe.wait_ge(probs1_ready, c * 6 + (i[0] + 1))
                elif name == "attended":
                    after("probsT", (i, 1))
                    if i == 0:
                        pe.wait_ge(v1_ready, c + 1)
                elif name == "normT":
                    pe.wait_ge(x2n_ready, c + 1)
                elif name == "gate":
                    after("normT", 1)
                elif name == "position":
                    pe.wait_ge(chosen_ready, c + 1)
                if positive(count := ps.number(use) - (RING - 1)):
                    pe.wait_ge(ring_read, count)
                cols = slice(HALF * i, HALF * i + HALF) if isinstance(i, int) else None
                last = None
                if name in ("xT", "headsT", "x1T", "normT"):
                    src = {"xT": x_in, "headsT": heads, "x1T": x1n, "normT": rows}[name]
                    for j in range(3):
                        last = nc.tensor.transpose(bank[:, P * j:P * j + P], src[:, 3 * i + j, 0:P], ident[:])
                elif name == "group_mean":
                    last = mm(bank[:, 0:1], group_avg[:], gn_mv[:, 0:1], start=True, stop=True)
                elif name == "group_var":
                    last = mm(bank[:, 0:1], group_avg[:], gn_small[:, 2:3], start=True, stop=True)
                elif name in ("q", "k"):
                    last = mm(bank[:, 0:HALF], (wq0 if name == "q" else wk0)[:], xnT[:, cols], start=True, stop=True)
                elif name in ("v", "V"):
                    src, w = (xnT, wv0) if name == "v" else (x1nT, wv1T)
                    for j in range(3):
                        tb = 3 * i + j
                        last = mm(bank[:, P * j:P * j + P], src[:, P * tb:P * tb + P], w[:], start=True, stop=True)
                elif name == "max":
                    h, qb, lo, n_ = MAX_UNITS[i]
                    last = mm(bank[:, 0:n_], q_max[:, h, P * qb:P * qb + P], k_max[:, h, lo:lo + n_],
                              start=True, stop=True)
                elif name == "maxT":
                    last = nc.tensor.transpose(bank[:, 0:P], neg_max[:], ident[:])
                elif name == "heads":
                    for quad in range(2):
                        last = nc.tensor.transpose(bank[:, P * quad:P * quad + P],
                                                   headsT_raw[:, quad, P * i:P * i + P], ident[:])
                elif name == "project":
                    for j in range(3):
                        tb = 3 * i + j
                        last = mm(bank[:, P * j:P * j + P], headsT[:, P * tb:P * tb + P], wo0[:], start=True, stop=True)
                elif name in ("A", "B"):
                    last = mm(bank[:, 0:HALF], (map_a if name == "A" else map_b)[:], x1nT[:, cols],
                              start=True, stop=True)
                elif name == "probsT":
                    for j in range(3):
                        kb = 3 * i[1] + j
                        last = nc.tensor.transpose(bank[:, P * j:P * j + P], probs1[:, P * kb:P * kb + P], ident[:])
                elif name == "attended":
                    for kb in range(TB):
                        last = mm(bank[:, 0:P], probs1T[:, P * kb:P * kb + P], v1[:, kb, :],
                                  start=(kb == 0), stop=(kb == TB - 1))
                elif name == "gate":
                    for tb in range(TB):
                        last = mm(bank[:, E * tb:E * tb + E], x2nT[:, P * tb:P * tb + P], gateT[:], start=True, stop=True)
                elif name == "position":
                    n_ = TB * E
                    mm(bank[:, 0:n_], before_mid[:], chosen[:].rearrange("p b e -> p (b e)"), start=True, stop=False,
                       skip_group_check=True)
                    for tb in range(TB):
                        for other in range(TB):
                            if other != tb:
                                mm(bank[:, E * tb:E * tb + E], (before_le if other < tb else before_lt)[:],
                                   chosen[:, other, :], start=False, stop=False, skip_group_check=True)
                    for tb in range(TB):
                        last = mm(bank[:, n_:n_ + E], ones_bf[:], chosen[:, tb, :], start=False, stop=(tb == TB - 1),
                                  skip_group_check=True)
                last.then_inc(ring_filled, 1)

            def body(ps):
                for t in range(TICKS):
                    d = t - 1
                    stage, q = ("add", t - 1) if t else ("end", TICKS - 1)
                    scoring = ps.has("mid") and 0 <= d < len(STEPS)
                    weighing = ps.has("mid") and 0 <= d - 1 < len(STEPS)
                    for i, part in enumerate(tick_order(t)):
                        if i in (0, 2) and scoring:
                            fill_scores(ps.batch("mid"), d, i // 2)
                        if i in (1, 3) and ps.has(stage) and q % 4:
                            add_logits(ps.batch(stage), q, i // 2)
                        if i in (3, 4) and ps.has(stage) and q % 4 == 0:
                            add_logits(ps.batch(stage), q, i - 3)
                        if i == 4 and weighing:
                            weigh_values(ps.batch("mid"), d - 1)
                        for use in part:
                            if ps.has(use[0]):
                                fill(ps, use)

            passes(pe, body)
            expert_products(pe)

        @block.vector
        def _(dve):
            v = nc.vector

            def rsqrt(y, var, tmp):
                dve.drain()
                v.tensor_scalar(y.bitcast(I32), var.bitcast(I32), -0.5, float(0x5F3759DF), ALU.mult, ALU.add)
                dve.drain()
                for _ in range(3):
                    v.scalar_tensor_tensor(tmp, y, -0.5, y, ALU.mult, ALU.mult)
                    dve.drain()
                    v.tensor_tensor(tmp, tmp, var, ALU.mult)
                    dve.drain()
                    v.scalar_tensor_tensor(y, tmp, 1.5, y, ALU.add, ALU.mult)
                    dve.drain()

            v.memset(xnT[0:96, 0:64 * H], 0.0).then_inc(setup_dve, 1)
            dve.wait_ge(tables_in, 16 * 8)
            dve.wait_ge(made, 1)
            v.tensor_copy(tn_hi, xnT[0:96, 0:64 * H].rearrange("p (w h) -> p w h", h=H))
            dve.drain()
            v.tensor_tensor(xT[0:96, 0:64 * H], xnT[0:96, 0:64 * H], tn_hi.rearrange("p w h -> p (w h)"), ALU.subtract)
            dve.drain()
            v.tensor_copy(tn_mid, xT[0:96, 0:64 * H].rearrange("p (w h) -> p w h", h=H))
            dve.drain()
            v.tensor_tensor(tn_lo, xT[0:96, 0:64 * H].rearrange("p (w h) -> p w h", h=H), tn_mid, ALU.subtract)
            dve.drain()
            for g, tab in enumerate((tn_hi, tn_mid, tn_lo)):
                rows_g = slice(32 * g, 32 * g + 32)
                for h in range(H):
                    for ub in range(TB):
                        hi = 47 - 8 * ub
                        t_part = tab[rows_g, hi - 7:hi + 1, h][:, ::-1].unsqueeze(1).to_broadcast([32, 16, 8])
                        n_part = tab[rows_g, 48:64, h][:, ::-1].unsqueeze(2).to_broadcast([32, 16, 8])
                        v.tensor_tensor(bias_q[rows_g, h, P * ub:P * ub + P].rearrange("p (n t) -> p n t", t=8),
                                        t_part, n_part, ALU.add)
            dve.drain()
            v.memset(gn_small[:, 0:1], 0.0).then_inc(setup_dve, 1)
            dve.wait_ge(weights_in, 16 * 27)
            dve.wait_ge(setup_pe, 1)
            v.tensor_copy(wv1T[:], ring[:, 0, 0:P])
            v.tensor_copy(w1T, ring[:, 0, P:P + 2 * HID].rearrange("p (a h) -> p a h", a=2))
            v.tensor_copy(gateT[:], ring[:, 0, 192:192 + E])
            v.tensor_copy(eb1T[:], ring[:, 0, 256:288])
            dve.drain()
            for a in range(2):
                v.tensor_copy(w1T_rep[:, a], w1T[:, a].unsqueeze(1).to_broadcast([P, 8, HID]))
            for k in range(4):
                v.tensor_scalar(w2_shifted[:, k, 8 * k:8 * k + 8], mask8[:], w2_col, None, ALU.mult)
            dve.drain()
            v.memset(gn_small[:, 0:1], 0.0).then_inc(setup_dve, 1)
            dve.wait_ge(setup_pe, 2)
            v.tensor_copy(map_a[:], av_bank[:, 0:P])
            v.tensor_copy(map_b[:], av_bank[:, P:2 * P])
            dve.drain()
            v.memset(gn_small[:, 0:1], 0.0).then_inc(setup_dve, 1)

            def sums(b, q):
                if positive(count := b * 24 + (q - 2)):
                    dve.wait_ge(logits_added, count)
                col = a_col(q, 0)
                v.tensor_scalar(hidden[:, q % 3, 0, :], b_rep[:], a_cols[:, col:col + 1], None, ALU.add) \
                 .then_inc(sums_dve, 1)

            def layer_norm(src, dst, done):
                for tb in range(TB):
                    v.bn_stats(ln_stats[:, tb, :], src[:, tb, :])
                dve.drain()
                for tb in range(TB):
                    v.bn_aggr(ln_mv[:, tb, :], ln_stats[:, tb, :])
                dve.drain()
                v.tensor_scalar(ln_small[:, 0, :], ln_mv[:, :, 1], 1e-5, None, ALU.add)
                rsqrt(ln_small[:, 1, :], ln_small[:, 0, :], ln_small[:, 2, :])
                for tb in range(TB):
                    last = v.tensor_scalar(dst[:, tb, 0:P], src[:, tb, :], ln_mv[:, tb, 0:1], ln_small[:, 1, tb:tb + 1],
                                           ALU.subtract, ALU.mult)
                last.then_inc(done, 1)

            def read(ps, use):
                stage, name, i = use
                c = ps.batch(stage)
                bank = ring[:, ps.bank(use)]
                cols = slice(HALF * i, HALF * i + HALF) if isinstance(i, int) else None
                if name == "A":
                    dve.drain()
                dve.wait_ge(ring_filled, ps.number(use) + 1)
                if name == "xT":
                    v.tensor_copy(xT[:, cols], bank[:, 0:HALF])
                    v.bn_stats(gn_stats[:, i, :], bank[:, 0:HALF]).then_inc(ring_read, 1)
                    if i == 1:
                        dve.drain()
                        v.bn_aggr(gn_mv[:], gn_stats[:].rearrange("p a s -> p (a s)")).then_inc(mean_ready, 1)
                elif name == "group_mean":
                    v.tensor_copy(gn_small[:, 0:1], bank[:, 0:1]).then_inc(ring_read, 1)
                    dve.drain()
                    v.tensor_tensor(gn_small[:, 1:2], gn_mv[:, 0:1], gn_small[:, 0:1], ALU.subtract)
                    dve.drain()
                    v.scalar_tensor_tensor(gn_small[:, 2:3], gn_small[:, 1:2], gn_small[:, 1:2], gn_mv[:, 1:2],
                                           ALU.mult, ALU.add).then_inc(var_ready, 1)
                elif name == "group_var":
                    v.tensor_scalar(gn_small[:, 3:4], bank[:, 0:1], 1e-5, None, ALU.add).then_inc(ring_read, 1)
                    rsqrt(gn_small[:, 4:5], gn_small[:, 3:4], gn_small[:, 5:6])
                    v.tensor_scalar(xnT[:], xT[:], gn_small[:, 0:1], gn_small[:, 4:5], ALU.subtract, ALU.mult) \
                     .then_inc(xn_ready, 1)
                elif name in ("q", "k"):
                    w, scale = (0, HD ** -0.5) if name == "q" else (1, 1.0)
                    if i == 0:
                        if positive(count := c * 16):
                            dve.wait_ge(parts_stored, count)
                        if positive(count := c * 2):
                            dve.wait_ge(parts_ready, count)
                    v.tensor_scalar(qk_parts[:, w, 0, cols], bank[:, 0:HALF], scale, None, ALU.mult)
                    dve.drain()
                    last = v.scalar_tensor_tensor(qk_rest[w][:, cols], bank[:, 0:HALF], scale, qk_parts[:, w, 0, cols],
                                                  ALU.mult, ALU.subtract)
                    last.then_inc(ring_read, 1)
                elif name == "v":
                    if i == 0:
                        if positive(count := c):
                            dve.wait_ge(v_aug_ready, count)
                    v.tensor_copy(v_next[:, 3 * i:3 * i + 3, :], bank[:, 0:HALF].rearrange("p (b c) -> p b c", b=3)) \
                     .then_inc(ring_read, 1)
                elif name == "max":
                    h, qb, lo, n_ = MAX_UNITS[i]
                    part = MAX_PARTS.index((qb, lo, n_))
                    v.tensor_reduce(max_halves[:, h, part:part + 1], bank[:, 0:n_], AX.X, ALU.max, negate=True) \
                     .then_inc(ring_read, 1)
                    if i == len(MAX_UNITS) - 1:
                        by_head = neg_max[:, 0:H * TB].rearrange("p (h q) -> p h q", q=TB)
                        dve.drain()
                        v.tensor_copy(by_head[:, :, 0:4], max_halves[:, :, 0:4])
                        v.tensor_reduce(by_head[:, :, 4], max_halves[:, :, 4:6], AX.X, ALU.min)
                        v.tensor_reduce(by_head[:, :, 5], max_halves[:, :, 6:9], AX.X, ALU.min)
                        dve.drain()
                        v.memset(gn_small[:, 6:7], 0.0).then_inc(max_done, 1)
                elif name == "maxT":
                    if positive(count := c * 48):
                        dve.wait_ge(max_rows_loaded, count)
                    n_ = H * TB
                    v.tensor_copy(max_parts[:, 0, :], bank[0:n_, 0:P])
                    dve.drain()
                    v.tensor_tensor(max_rest, bank[0:n_, 0:P], max_parts[:, 0, :], ALU.subtract).then_inc(ring_read, 1)
                    dve.drain()
                    v.tensor_copy(max_parts[:, 1, :], max_rest)
                    dve.drain()
                    v.tensor_tensor(max_parts[:, 2, :], max_rest, max_parts[:, 1, :], ALU.subtract) \
                     .then_inc(max_parts_ready, 1)
                elif name == "heads":
                    by_head = bank[:, 0:2 * P].rearrange("p (h d) -> p h d", d=32)
                    v.reciprocal(head_scale[:, i % 2], by_head[:, :, 16])
                    dve.drain()
                    v.tensor_tensor(heads[:, i, :].rearrange("p (h d) -> p h d", d=HD), by_head[:, :, 0:HD],
                                    head_scale[:, i % 2].unsqueeze(2).to_broadcast([P, H, HD]), ALU.mult) \
                     .then_inc(ring_read, 1)
                elif name in ("headsT", "x1T", "normT"):
                    dst = {"headsT": headsT, "x1T": x1nT, "normT": x2nT}[name]
                    v.tensor_copy(dst[:, cols], bank[:, 0:HALF]).then_inc(ring_read, 1)
                elif name == "project":
                    if i == 0:
                        dve.wait_ge(res_loaded, c * 96 + 96)
                    v.tensor_tensor(x1_next[:, 3 * i:3 * i + 3, :], bank[:, 0:HALF].rearrange("p (b c) -> p b c", b=3),
                                    x1_next[:, 3 * i:3 * i + 3, :], ALU.add).then_inc(ring_read, 1)
                    if i == 1:
                        dve.drain()
                        layer_norm(x1_next, x1n, x1n_ready)
                elif name == "A":
                    v.tensor_tensor(a_masked.rearrange("p (o i) -> p o i", i=8),
                                    bank[:, 0:HALF].rearrange("p (o i) -> p o i", i=8),
                                    mask8[:].unsqueeze(1).to_broadcast([P, HALF // 8, 8]), ALU.mult) \
                     .then_inc(ring_read, 1)
                    dve.drain()
                    v.tensor_reduce(a_next[:, 48 * i:48 * i + 48], a_masked.rearrange("p (o i) -> p o i", i=8),
                                    AX.X, ALU.add)
                elif name == "B":
                    v.tensor_scalar(b_next[:, cols], bank[:, 0:HALF], b1_col[:], None, ALU.add).then_inc(ring_read, 1)
                elif name == "V":
                    if i == 0:
                        if positive(count := c):
                            dve.wait_ge(v1_ready, count)
                    v.tensor_copy(v1_next[:, 3 * i:3 * i + 3, :], bank[:, 0:HALF].rearrange("p (b c) -> p b c", b=3)) \
                     .then_inc(ring_read, 1)
                elif name == "probsT":
                    s_, half = i
                    v.tensor_copy(probs1T[:, HALF * half:HALF * half + HALF], bank[:, 0:HALF]).then_inc(ring_read, 1)
                elif name == "attended":
                    v.reciprocal(row_scale[:, i % 2:i % 2 + 1], row_sum[:])
                    dve.drain()
                    if positive(count := c * 96 - 96 + 16 * (i + 1)):
                        dve.wait_ge(x2_stored, count)
                    if i == 0:
                        dve.wait_ge(x1_kept, c + 1)
                    v.scalar_tensor_tensor(x2[:, i, :], bank[:, 0:P], row_scale[:, i % 2:i % 2 + 1], x1[:, i, :], ALU.mult, ALU.add) \
                     .then_inc(ring_read, 1)
                elif name == "gate":
                    g_ = bank[:, 0:TB * E].rearrange("p (b e) -> p b e", e=E)
                    v.tensor_reduce(rs[:, 0, 0, :], g_, AX.X, ALU.max)
                    dve.drain()
                    v.tensor_tensor(rt[:, 0], g_, rs[:, 0, 0, :].unsqueeze(2).to_broadcast([P, TB, E]),
                                    ALU.subtract).then_inc(ring_read, 1)
                elif name == "position":
                    assign_slots(c, bank)

            def over_e(col):
                return col.unsqueeze(2).to_broadcast([P, TB, E])

            def over_b(row):
                return row.unsqueeze(1).to_broadcast([P, TB, E])

            def choose(c):
                probs, first, second = rt[:, 2], rt[:, 4], rt[:, 5]
                dve.wait_ge(gate_exp, c + 1)
                v.tensor_reduce(rs[:, 1, 0, :], rt[:, 1], AX.X, ALU.add)
                dve.drain()
                v.reciprocal(rs[:, 2, 0, :], rs[:, 1, 0, :])
                dve.drain()
                v.tensor_tensor(probs, rt[:, 1], over_e(rs[:, 2, 0, :]), ALU.mult)
                dve.drain()
                for k, (src, hot) in enumerate(((probs, first), (rt[:, 6], second))):
                    v.tensor_reduce(rs[:, 3, k, :], src, AX.X, ALU.max)
                    dve.drain()
                    v.tensor_tensor(rt[:, 3], src, over_e(rs[:, 3, k, :]), ALU.is_equal)
                    dve.drain()
                    v.tensor_tensor(rt[:, 3], rt[:, 3], over_b(tie_rank[:]), ALU.mult)
                    dve.drain()
                    v.tensor_reduce(rs[:, 4, k, :], rt[:, 3], AX.X, ALU.max)
                    dve.drain()
                    v.tensor_tensor(hot, over_b(tie_rank[:]), over_e(rs[:, 4, k, :]), ALU.is_equal)
                    dve.drain()
                    if k == 0:
                        v.scalar_tensor_tensor(rt[:, 6], first, -2.0, probs, ALU.mult, ALU.add)
                        dve.drain()
                v.tensor_tensor(chosen[:], first, second, ALU.add).then_inc(chosen_ready, 1)

            def assign_slots(c, bank):
                n_ = TB * E
                v.tensor_tensor(rt[:, 7], bank[:, 0:n_].rearrange("p (b e) -> p b e", e=E), over_b(counts[:]), ALU.add)
                dve.drain()
                v.tensor_tensor(counts[:], counts[:], bank[:, n_:n_ + E], ALU.add).then_inc(ring_read, 1)
                for k in range(2):
                    v.tensor_tensor(rt[:, 8 + k], rt[:, 7], rt[:, 4 + k], ALU.mult)
                    v.tensor_tensor(rt[:, 10 + k], rt[:, 4 + k], over_b(expert_ids[:]), ALU.mult)
                v.tensor_tensor(rs[:, 5, 0, :], rs[:, 3, 0, :], rs[:, 3, 1, :], ALU.add)
                dve.drain()
                for k in range(2):
                    v.tensor_reduce(rs[:, 6, k, :], rt[:, 8 + k], AX.X, ALU.add)
                    v.tensor_reduce(rs[:, 7, k, :], rt[:, 10 + k], AX.X, ALU.add)
                v.reciprocal(rs[:, 5, 1, :], rs[:, 5, 0, :])
                dve.drain()
                v.tensor_scalar(rs[:, 8], rs[:, 6], float(CAP), float(NOWHERE), ALU.is_ge, ALU.mult)
                v.scalar_tensor_tensor(rs[:, 9], rs[:, 7], float(CAP), rs[:, 6], ALU.mult, ALU.add)
                v.tensor_tensor(rows[:, :, 129], rs[:, 3, 0, :], rs[:, 5, 1, :], ALU.mult)
                v.tensor_tensor(rows[:, :, 131], rs[:, 3, 1, :], rs[:, 5, 1, :], ALU.mult)
                v.tensor_copy(rows[:, :, 130], rs[:, 7, 0, :])
                v.tensor_copy(rows[:, :, 128].bitcast(I32), token_ids[:])
                dve.drain()
                v.tensor_tensor(slots[:], rs[:, 8], rs[:, 9], ALU.add).then_inc(slots_ready, 1)
                v.tensor_scalar(token_ids[:], token_ids[:], float(L), None, ALU.add)

            v.tensor_scalar(rt[:, 0:2, :, :].rearrange("p a b e -> p (a b e)")[:, 0:16], ids_int[:, 0:16], 0.0, None,
                            ALU.is_ge)
            v.tensor_scalar(rs[:, 0, 0, :], ids_int[:, 16:16 + TB], -40.0, None, ALU.add)
            v.tensor_copy(expert_ids[:], ids_int[:, 24:32])
            v.tensor_copy(tie_rank[:], ids_int[:, 32:40])
            dve.drain()
            v.tensor_reduce(rs[:, 1, 0, 0:1], rt[:, 0:2, :, :].rearrange("p a b e -> p (a b e)")[:, 0:16], AX.X, ALU.add)
            dve.drain()
            v.scalar_tensor_tensor(token_ids[:], rs[:, 1, 0, 0:1].to_broadcast([P, TB]), 40.0, rs[:, 0, 0, :],
                                   ALU.mult, ALU.add)
            dve.drain()

            def body(ps):
                for t in range(TICKS):
                    parts = tick_order(t)
                    if t == 0 and ps.has("add"):
                        b = ps.batch("add")
                        dve.drain()
                        if positive(count := b * 24 - 1):
                            dve.wait_ge(tanh_done, count)
                        if positive(count := b * 24):
                            dve.wait_ge(sums_pool, count)
                        v.tensor_copy(a_cols[:], a_next[:])
                        dve.drain()
                        v.tensor_copy(b_rep[:], b_next[:]).then_inc(ab_ready, 1)
                        dve.drain()
                        sums(b, 0)
                    if ps.has("add") and t < TICKS - 1:
                        sums(ps.batch("add"), t + 1)
                    if ps.has("mid") and t - 3 in LAST_OF_GROUP:
                        c, d = ps.batch("mid"), t - 3
                        quad, lo = STEPS[d][:2]
                        dve.wait_ge(av_done, c * 18 + (d + 1))
                        v.tensor_copy(headsT_raw[:, quad, lo:lo + HALF], av_bank[:, 0:HALF]).then_inc(av_copied, 1)
                    if ps.has("end") and t == 7:
                        choose(ps.batch("end"))
                    for use in parts[0] + parts[1] + parts[2]:
                        if ps.has(use[0]):
                            read(ps, use)
                    if ps.has("end") and t == 3:
                        c = ps.batch("end")
                        dve.drain()
                        dve.wait_ge(rows_sent, 16 + c * 192)
                        layer_norm(x2, rows, x2n_ready)
                    stage, blk = ("add", t // 4 - 1) if t else ("end", 5)
                    if t % 4 == 0 and ps.has(stage) and blk >= 0:
                        c = ps.batch(stage)
                        if blk == 0 and not positive(c):
                            dve.wait_ge(rows_sent, 16)
                        dve.wait_ge(logits_added, c * 24 + 4 * (blk + 1))
                        if positive(count := c * 6 + blk):
                            dve.wait_ge(probs1_ready, count)
                        v.tensor_reduce(logit_bias[:, 0:1], logits[:, :, 0:HALF], AX.XY, ALU.max)
                        dve.drain()
                        v.tensor_scalar(logit_bias[:, 1:2], logit_bias[:, 0:1], b2_col[:], -1.0, ALU.add, ALU.mult)
                        dve.drain()
                        v.tensor_scalar(logit_bias[:, 2:3], logit_bias[:, 1:2], b2_col[:], None, ALU.add) \
                         .then_inc(max1_ready, 1)
                    for use in parts[3] + parts[4]:
                        if ps.has(use[0]):
                            read(ps, use)

            passes(dve, body)
            expert_vector(dve)


_INS = ['x', 'L0_conv_Wq', 'L0_conv_Wk', 'L0_conv_Wv', 'L0_conv_Wo', 'L0_conv_rel_pos_bias',
        'L0_conv_particle_rel_pos_bias', 'L1_attn_Wq', 'L1_attn_Wk', 'L1_attn_Wv', 'L1_attn_W1', 'L1_attn_b1',
        'L1_attn_w2', 'L1_attn_b2', 'L1_ffn_gate_w', 'L1_ffn_w1', 'L1_ffn_b1', 'L1_ffn_w2', 'L1_ffn_b2']


def kernel(**inputs):
    import numpy as _np
    import concourse.bacc as _bacc
    from concourse import mybir as _mybir
    from concourse.bass_utils import run_bass_kernel_spmd as _run

    nc = _bacc.Bacc("TRN2", target_bir_lowering=False, num_devices=1)
    arrays, args = {}, []
    for name in _INS:
        a = _np.ascontiguousarray(inputs[name])
        arrays[f"in_{name}_dram"] = a
        args.append(nc.dram_tensor(f"in_{name}_dram", a.shape, _mybir.dt.from_np(a.dtype), kind="ExternalInput").ap())
    args.append(nc.dram_tensor("out_0_dram", inputs['x'].shape, F32, kind="ExternalOutput").ap())
    hybrid_kernel(nc, *args)
    r = _run(nc, [arrays], core_ids=[0])
    return r.results[0]["out_0_dram"]
```
